# Optimizing a Trainium2 kernel written in Bass

```python
import numpy as np
import jax
import jax.numpy as jnp

def _softmax(x, axis=-1):
    return jax.nn.softmax(x, axis=axis)

def _gelu(x):
    return jax.nn.gelu(x, approximate=True)

def _silu(x):
    return jax.nn.silu(x)

def _sigmoid(x):
    return jax.nn.sigmoid(x)

def _layernorm(x, axis=-1, eps=1e-05):
    m = jnp.mean(x, axis=axis, keepdims=True)
    v = jnp.var(x, axis=axis, keepdims=True)
    return (x - m) / jnp.sqrt(v + eps)

def _scatter_add(tgt, idx, src, axis=0):
    return tgt.at[idx].add(src)

def _segment_sum(src, seg, n):
    return jax.ops.segment_sum(src, seg, n)
kernel_name = 'mk_adaln_attn_ffn_d1_seqx_r4_40f01f'

def setup_inputs(seed: int=0):
    np.random.seed(seed)
    _w = jnp.asarray

    def _rec_inputs():
        import jax
        import jax.numpy as jnp
        _rk = jax.random.key(seed)
        x = -0.0002928 + 1 * jax.random.normal(jax.random.fold_in(_rk, 1), (2, 1024, 256), jnp.float32)
        _lenS = 1024 - jax.random.randint(jax.random.fold_in(_rk, 7), (2,), 0, max(1, 1024 // 4) + 1, jnp.int32)
        _lenS2 = 1024 - jax.random.randint(jax.random.fold_in(_rk, 8), (2,), 0, max(1, 1024 // 4) + 1, jnp.int32)
        fside_16xSxS_0 = -5.72187e-05 + 0.999849 * jax.random.normal(jax.random.fold_in(_rk, 11), (16, 1024, 1024), jnp.float32)
        cond_64 = -0.0265395 + 0.99382 * jax.random.normal(jax.random.fold_in(_rk, 13), (2, 64), jnp.float32)
        _validS = jnp.arange(1024)[None, :] < _lenS[:, None]
        _validS2 = jnp.arange(1024)[None, :] < _lenS2[:, None]
        _causal = jnp.tril(jnp.ones((1024, 1024), dtype=bool))
        mask_BxS_bk0 = jnp.logical_not(jnp.broadcast_to(_validS[:, :], (2, 1024)))
        return (x, fside_16xSxS_0, cond_64, mask_BxS_bk0)
    x, fside_16xSxS_0, cond_64, mask_BxS_bk0 = _rec_inputs()

    def _L0_cond_setup():
        import jax, jax.numpy as jnp
        import numpy as np
        B, N, DIM, H, DH = (2, 512, 256, 16, 64)
        INNER = H * DH
        EPS = 1e-05

        def layernorm(x, g):
            mean = jnp.mean(x, axis=-1, keepdims=True)
            var = jnp.var(x, axis=-1, keepdims=True)
            return (x - mean) * jax.lax.rsqrt(var + EPS) * g
        key = jax.random.key(seed)
        ks = jax.random.split(key, 10)
        x = jax.random.normal(ks[0], (B, N, DIM), dtype=jnp.float32)
        attn_bias = jax.random.normal(ks[1], (H, N, N), dtype=jnp.float32)
        mask = jax.random.randint(ks[2], (B, N), 0, 2).astype(bool)
        g_in = jnp.ones((DIM,), dtype=jnp.float32)
        null_attn_bias = jax.random.normal(ks[3], (H,), dtype=jnp.float32)
        null_kv = jax.random.normal(ks[4], (2, DH), dtype=jnp.float32)
        Wq = jax.random.normal(ks[5], (DIM, INNER), dtype=jnp.float32) * 0.02
        Wkv = jax.random.normal(ks[6], (DIM, 2 * DH), dtype=jnp.float32) * 0.02
        Wo = jax.random.normal(ks[7], (INNER, DIM), dtype=jnp.float32) * 0.02
        g_out = jnp.ones((DIM,), dtype=jnp.float32)
        return {'x': x, 'attn_bias': attn_bias, 'mask': mask, 'g_in': g_in, 'null_attn_bias': null_attn_bias, 'null_kv': null_kv, 'Wq': Wq, 'Wkv': Wkv, 'Wo': Wo, 'g_out': g_out}
    _L0_cond_all = _L0_cond_setup()
    _L0_cond_in = {k: v for k, v in _L0_cond_all.items() if k in ('g_in', 'null_attn_bias', 'Wq', 'Wkv', 'Wo', 'g_out')}
    del _L0_cond_all

    def _L0_attn_setup():
        import jax, jax.numpy as jnp
        import numpy as np
        import math
        HID_DIM = 256
        NUM_HEADS = 8
        QK_DIM = HID_DIM // 8
        key = jax.random.key(seed)
        ks = jax.random.split(key, 7)
        B, M, C = (4, 512, HID_DIM)
        gain = math.sqrt(2.0)

        def xavier(k, fan_in, fan_out):
            std = gain * math.sqrt(2.0 / (fan_in + fan_out))
            a = math.sqrt(3.0) * std
            return jax.random.uniform(k, (fan_out, fan_in), jnp.float32, -a, a)
        x = jax.random.normal(ks[0], (B, M, C), jnp.float32)
        Wq = xavier(ks[1], C, QK_DIM)
        Wk = xavier(ks[2], C, QK_DIM)
        Wv = xavier(ks[3], C, C)
        bq = jnp.zeros((QK_DIM,), jnp.float32)
        bk = jnp.zeros((QK_DIM,), jnp.float32)
        bv = jnp.zeros((C,), jnp.float32)
        gamma = jnp.zeros((1,), jnp.float32)
        return {'x': x, 'Wq': Wq, 'bq': bq, 'Wk': Wk, 'bk': bk, 'Wv': Wv, 'bv': bv, 'gamma': gamma}
    _L0_attn_all = _L0_attn_setup()
    _L0_attn_in = {k: v for k, v in _L0_attn_all.items() if k in ('Wq', 'bq', 'Wk', 'bk', 'Wv', 'bv', 'gamma')}
    del _L0_attn_all

    def _L0_cond2_setup():
        import jax, jax.numpy as jnp
        import numpy as np
        B, S, H = (4, 512, 256)
        E = 8
        M = 128
        K = 2
        N_SHARED = 2
        SM = M * N_SHARED
        G = 64
        GE_TEMP = 1.0
        ALPHA = 0.001
        SEQ_AUX = True
        NORM_TOPK = True
        COS_TEMP = 0.78
        CONS_ALPHA = 0.01
        LEAKY_SLOPE = 0.01
        EPS_COS = 1e-08

        def _leaky(x):
            return jnp.where(x >= 0, x, LEAKY_SLOPE * x)

        def _moe_forward(hidden_states, g, wt, wg, w_gate, w_up, w_down, sw_gate, sw_up, sw_down):
            b, s, h = hidden_states.shape
            x = hidden_states.reshape(-1, h)
            T = x.shape[0]
            logits_h = x @ wt.T
            logits_g = g @ wg.T
            logits_g = jnp.repeat(logits_g, s, axis=0)
            logits = (logits_h + logits_g / GE_TEMP) / (1.0 + 1.0 / GE_TEMP)
            scores = jax.nn.softmax(logits, axis=-1)
            topk_w, topk_idx = jax.lax.top_k(scores, K)
            if K > 1 and NORM_TOPK:
                topk_w = topk_w / (topk_w.sum(-1, keepdims=True) + 1e-20)
            onehot = jax.nn.one_hot(topk_idx.reshape(b, s * K), E, dtype=jnp.float32)
            ce = onehot.sum(1) / (s * K / E)
            aux_loss = (ce * scores.reshape(b, s, E).mean(1)).sum(1).mean() * ALPHA
            gp = _leaky(jnp.einsum('th,ehm->etm', x, w_gate))
            up = jnp.einsum('th,ehm->etm', x, w_up)
            y_all = jnp.einsum('etm,emh->eth', gp * up, w_down)
            y_sel = y_all[topk_idx, jnp.arange(T)[:, None], :]
            y = (y_sel * topk_w[..., None]).sum(1).reshape(b, s, h)
            p = _leaky(hidden_states @ sw_gate) * (hidden_states @ sw_up) @ sw_down
            y = y + p
            num = jnp.sum(y * p, -1)
            den = jnp.maximum(jnp.linalg.norm(y, axis=-1), EPS_COS) * jnp.maximum(jnp.linalg.norm(p, axis=-1), EPS_COS)
            closs = CONS_ALPHA * jnp.mean(num / den / (1.0 + COS_TEMP))
            return (y, aux_loss + closs)
        key = jax.random.key(seed)
        ks = jax.random.split(key, 12)
        sh = 1.0 / np.sqrt(H)
        sm = 1.0 / np.sqrt(M)
        ssm = 1.0 / np.sqrt(SM)
        sg = 1.0 / np.sqrt(G)
        return {'hidden_states': jax.random.normal(ks[0], (B, S, H), jnp.float32), 'g': jax.random.normal(ks[1], (B, G), jnp.float32), 'wt': jax.random.uniform(ks[2], (E, H), jnp.float32, -sh, sh), 'wg': jax.random.uniform(ks[3], (E, G), jnp.float32, -sg, sg), 'w_gate': jax.random.uniform(ks[4], (E, H, M), jnp.float32, -sh, sh), 'w_up': jax.random.uniform(ks[5], (E, H, M), jnp.float32, -sh, sh), 'w_down': jax.random.uniform(ks[6], (E, M, H), jnp.float32, -sm, sm), 'sw_gate': jax.random.uniform(ks[7], (H, SM), jnp.float32, -sh, sh), 'sw_up': jax.random.uniform(ks[8], (H, SM), jnp.float32, -sh, sh), 'sw_down': jax.random.uniform(ks[9], (SM, H), jnp.float32, -ssm, ssm)}
    _L0_cond2_all = _L0_cond2_setup()
    _L0_cond2_in = {k: v for k, v in _L0_cond2_all.items() if k in ('wt', 'wg', 'w_gate', 'w_up', 'w_down', 'sw_gate', 'sw_up', 'sw_down')}
    del _L0_cond2_all

    def _L0_ffn_setup():
        import jax, jax.numpy as jnp
        import numpy as np
        CAPACITY_RATIO = 0.75
        key = jax.random.key(seed)
        k1, k2, k3 = jax.random.split(key, 3)
        B, L, D = (4, 2048, 256)
        x = jax.random.normal(k1, (B, L, D), dtype=jnp.float32)
        w_router = jax.random.normal(k2, (D,), dtype=jnp.float32) * 0.02
        w_block = jax.random.normal(k3, (D, D), dtype=jnp.float32) * 0.02
        return {'x': x, 'w_router': w_router, 'w_block': w_block}
    _L0_ffn_all = _L0_ffn_setup()
    _L0_ffn_in = {k: v for k, v in _L0_ffn_all.items() if k in ('w_router', 'w_block')}
    del _L0_ffn_all
    return {'x': x, 'fside_16xSxS_0': fside_16xSxS_0, 'cond_64': cond_64, 'mask_BxS_bk0': mask_BxS_bk0, 'L0_cond_g_in': _L0_cond_in['g_in'], 'L0_cond_null_attn_bias': _L0_cond_in['null_attn_bias'], 'L0_cond_Wq': _L0_cond_in['Wq'], 'L0_cond_Wkv': _L0_cond_in['Wkv'], 'L0_cond_Wo': _L0_cond_in['Wo'], 'L0_cond_g_out': _L0_cond_in['g_out'], 'L0_attn_Wq': _L0_attn_in['Wq'], 'L0_attn_bq': _L0_attn_in['bq'], 'L0_attn_Wk': _L0_attn_in['Wk'], 'L0_attn_bk': _L0_attn_in['bk'], 'L0_attn_Wv': _L0_attn_in['Wv'], 'L0_attn_bv': _L0_attn_in['bv'], 'L0_attn_gamma': _L0_attn_in['gamma'], 'L0_cond2_wt': _L0_cond2_in['wt'], 'L0_cond2_wg': _L0_cond2_in['wg'], 'L0_cond2_w_gate': _L0_cond2_in['w_gate'], 'L0_cond2_w_up': _L0_cond2_in['w_up'], 'L0_cond2_w_down': _L0_cond2_in['w_down'], 'L0_cond2_sw_gate': _L0_cond2_in['sw_gate'], 'L0_cond2_sw_up': _L0_cond2_in['sw_up'], 'L0_cond2_sw_down': _L0_cond2_in['sw_down'], 'L0_ffn_w_router': _L0_ffn_in['w_router'], 'L0_ffn_w_block': _L0_ffn_in['w_block']}

def reference(x, fside_16xSxS_0, cond_64, mask_BxS_bk0, L0_cond_g_in, L0_cond_null_attn_bias, L0_cond_Wq, L0_cond_Wkv, L0_cond_Wo, L0_cond_g_out, L0_attn_Wq, L0_attn_bq, L0_attn_Wk, L0_attn_bk, L0_attn_Wv, L0_attn_bv, L0_attn_gamma, L0_cond2_wt, L0_cond2_wg, L0_cond2_w_gate, L0_cond2_w_up, L0_cond2_w_down, L0_cond2_sw_gate, L0_cond2_sw_up, L0_cond2_sw_down, L0_ffn_w_router, L0_ffn_w_block):
    import jax
    import jax.numpy as jnp

    def _L0_cond_ref(x, attn_bias, mask, g_in, null_attn_bias, null_kv, Wq, Wkv, Wo, g_out):
        import jax, jax.numpy as jnp
        import numpy as np
        B, N, DIM, H, DH = (2, 512, 256, 16, 64)
        INNER = H * DH
        EPS = 1e-05

        def layernorm(x, g):
            mean = jnp.mean(x, axis=-1, keepdims=True)
            var = jnp.var(x, axis=-1, keepdims=True)
            return (x - mean) * jax.lax.rsqrt(var + EPS) * g
        b, n, _ = x.shape
        scale = DH ** (-0.5)
        xn = layernorm(x, g_in)
        q = (xn @ Wq).reshape(b, n, H, DH).transpose(0, 2, 1, 3) * scale
        kv = xn @ Wkv
        k, v = (kv[..., :DH], kv[..., DH:])
        nk = jnp.broadcast_to(null_kv[0], (b, 1, DH))
        nv = jnp.broadcast_to(null_kv[1], (b, 1, DH))
        k = jnp.concatenate([nk, k], axis=1)
        v = jnp.concatenate([nv, v], axis=1)
        sim = jnp.einsum('bhid,bjd->bhij', q, k)
        null_col = jnp.broadcast_to(null_attn_bias[:, None, None], (H, n, 1))
        bias = jnp.concatenate([null_col, attn_bias], axis=-1)
        sim = sim + bias
        neg = -jnp.finfo(sim.dtype).max
        j = n + 1
        causal_mask = jnp.triu(jnp.ones((n, j), dtype=bool), k=j - n + 1)
        sim = jnp.where(causal_mask, neg, sim)
        mask_p = jnp.pad(mask, ((0, 0), (1, 0)), constant_values=True)
        sim = jnp.where(mask_p[:, None, None, :], sim, neg)
        attn = jax.nn.softmax(sim, axis=-1)
        out = jnp.einsum('bhij,bjd->bhid', attn, v)
        out = out.transpose(0, 2, 1, 3).reshape(b, n, INNER)
        out = out @ Wo
        return layernorm(out, g_out)

    def _L0_attn_ref(x, Wq, bq, Wk, bk, Wv, bv, gamma):
        import jax, jax.numpy as jnp
        import numpy as np
        import math
        HID_DIM = 256
        NUM_HEADS = 8
        QK_DIM = HID_DIM // 8
        B, M, C = x.shape
        H = NUM_HEADS
        dqk = QK_DIM // H
        dv = C // H
        q = (x @ Wq.T + bq).reshape(B, M, H, dqk)
        k = (x @ Wk.T + bk).reshape(B, M, H, dqk)
        v = (x @ Wv.T + bv).reshape(B, M, H, dv)
        scores = jnp.einsum('bmhd,bnhd->bhmn', q, k) / math.sqrt(dqk)
        scores = jnp.where(scores >= 0, scores, 0.2 * scores)
        beta = jax.nn.softmax(scores, axis=-1)
        out = jnp.einsum('bhmn,bnhd->bmhd', beta, v).reshape(B, M, C)
        return gamma * out + x

    def _L0_cond2_ref(hidden_states, g, wt, wg, w_gate, w_up, w_down, sw_gate, sw_up, sw_down):
        import jax, jax.numpy as jnp
        import numpy as np
        B, S, H = (4, 512, 256)
        E = 8
        M = 128
        K = 2
        N_SHARED = 2
        SM = M * N_SHARED
        G = 64
        GE_TEMP = 1.0
        ALPHA = 0.001
        SEQ_AUX = True
        NORM_TOPK = True
        COS_TEMP = 0.78
        CONS_ALPHA = 0.01
        LEAKY_SLOPE = 0.01
        EPS_COS = 1e-08

        def _leaky(x):
            return jnp.where(x >= 0, x, LEAKY_SLOPE * x)

        def _moe_forward(hidden_states, g, wt, wg, w_gate, w_up, w_down, sw_gate, sw_up, sw_down):
            b, s, h = hidden_states.shape
            x = hidden_states.reshape(-1, h)
            T = x.shape[0]
            logits_h = x @ wt.T
            logits_g = g @ wg.T
            logits_g = jnp.repeat(logits_g, s, axis=0)
            logits = (logits_h + logits_g / GE_TEMP) / (1.0 + 1.0 / GE_TEMP)
            scores = jax.nn.softmax(logits, axis=-1)
            topk_w, topk_idx = jax.lax.top_k(scores, K)
            if K > 1 and NORM_TOPK:
                topk_w = topk_w / (topk_w.sum(-1, keepdims=True) + 1e-20)
            onehot = jax.nn.one_hot(topk_idx.reshape(b, s * K), E, dtype=jnp.float32)
            ce = onehot.sum(1) / (s * K / E)
            aux_loss = (ce * scores.reshape(b, s, E).mean(1)).sum(1).mean() * ALPHA
            gp = _leaky(jnp.einsum('th,ehm->etm', x, w_gate))
            up = jnp.einsum('th,ehm->etm', x, w_up)
            y_all = jnp.einsum('etm,emh->eth', gp * up, w_down)
            y_sel = y_all[topk_idx, jnp.arange(T)[:, None], :]
            y = (y_sel * topk_w[..., None]).sum(1).reshape(b, s, h)
            p = _leaky(hidden_states @ sw_gate) * (hidden_states @ sw_up) @ sw_down
            y = y + p
            num = jnp.sum(y * p, -1)
            den = jnp.maximum(jnp.linalg.norm(y, axis=-1), EPS_COS) * jnp.maximum(jnp.linalg.norm(p, axis=-1), EPS_COS)
            closs = CONS_ALPHA * jnp.mean(num / den / (1.0 + COS_TEMP))
            return (y, aux_loss + closs)
        y, _ = _moe_forward(hidden_states, g, wt, wg, w_gate, w_up, w_down, sw_gate, sw_up, sw_down)
        return y

    def _L0_ffn_ref(x, w_router, w_block):
        import jax, jax.numpy as jnp
        import numpy as np
        CAPACITY_RATIO = 0.75
        B, L, D = x.shape
        k = max(1, int(L * CAPACITY_RATIO))
        scores = jnp.einsum('bld,d->bl', x, w_router)
        _, top_idx = jax.lax.top_k(scores, k)
        selected = jnp.take_along_axis(x, top_idx[:, :, None], axis=1)
        processed = jax.nn.gelu(jnp.einsum('bkd,de->bke', selected, w_block))
        batch_idx = jnp.arange(B)[:, None]
        out = x.at[batch_idx, top_idx].set(processed)
        return out
    x = x + _L0_attn_ref(_L0_cond_ref(x, fside_16xSxS_0, mask_BxS_bk0, L0_cond_g_in, L0_cond_null_attn_bias, cond_64, L0_cond_Wq, L0_cond_Wkv, L0_cond_Wo, L0_cond_g_out), L0_attn_Wq, L0_attn_bq, L0_attn_Wk, L0_attn_bk, L0_attn_Wv, L0_attn_bv, L0_attn_gamma)
    x = x + _L0_ffn_ref(_L0_cond2_ref(x, cond_64, L0_cond2_wt, L0_cond2_wg, L0_cond2_w_gate, L0_cond2_w_up, L0_cond2_w_down, L0_cond2_sw_gate, L0_cond2_sw_up, L0_cond2_sw_down), L0_ffn_w_router, L0_ffn_w_block)
    return x

_drawn_inputs = setup_inputs


def setup_inputs(seed=0):
    import zlib

    import numpy as np

    out = dict(_drawn_inputs(seed))
    spreads = {'L0_cond_g_in': (1.0, 0.2),
     'L0_cond_g_out': (1.0, 0.2),
     'L0_attn_bq': (0.0, 0.1),
     'L0_attn_bk': (0.0, 0.1),
     'L0_attn_bv': (0.0, 0.1)}
    factors = {}
    for name, (base, spread) in spreads.items():
        noise = np.random.default_rng([zlib.crc32(name.encode()), seed]).standard_normal(out[name].shape)
        drawn = base * np.exp(spread * noise) if base else spread * noise
        out[name] = jnp.asarray(drawn.astype(out[name].dtype))
    for name, factor in factors.items():
        out[name] = (out[name] * factor).astype(out[name].dtype)
    return out
```

```python
from contextlib import ExitStack

import concourse.bass as bass
from concourse import mybir

F32 = mybir.dt.float32
BF16 = mybir.dt.bfloat16
U8 = mybir.dt.uint8
ALU = mybir.AluOpType
ACT = mybir.ActivationFunctionType
AX_X = mybir.AxisListType.X

P = 128
B, N, D = 2, 1024, 256
TB = N // P
NT = B * TB
KD = D // P
CH = 512
NC_ = B * N // CH
H1, DH = 16, 64
NP1 = H1 // 2
H2, DQ, DV = 8, 4, 32
E, M = 8, 128
SM = 256
G = 64
EPS = 1e-5
NEG = -1e30
TOPK = N * 3 // 4


def half_plan(kb0, UNR):
    nq = TB - kb0
    units, ring, halves = [], [], []
    for s in range(UNR):
        ring += [("q", s, b) for b in range(B)]
        for he in range(2):
            for qt in range(kb0, TB):
                for b in range(B):
                    units.append(dict(s=s, he=he, qt=qt, b=b, ring=len(ring), g=2 * s + he,
                                      first=qt == kb0, last=qt == TB - 1))
                    ring.append(("S", len(units) - 1))
    slot, count = 0, [0, 0]
    steps = {}
    for j in range(-2, len(units) + 5):
        mine = []
        if 0 <= j < len(units):
            u = units[j]
            blocks = list(range(kb0, u["qt"] + 1))
            for c in range(0, len(blocks), 4):
                mine.append(dict(kind="P", u=j, blocks=blocks[c:c + 4], slot=slot, first=c == 0,
                                 last=c + 4 >= len(blocks)))
                slot ^= 1
        e = j - 3
        if 0 <= e < len(units) and units[e]["he"] == 1 and units[e]["last"] and units[e]["b"] == B - 1:
            tiles = [(b, qt) for b in range(B) for qt in range(kb0, TB)]
            for c in range(0, len(tiles), 4):
                mine.append(dict(kind="O", s=units[e]["s"], g=units[e]["g"], tiles=tiles[c:c + 4], slot=slot))
                slot ^= 1
        for h in mine:
            count[h["slot"]] += 1
            h["n"] = count[h["slot"]]
        halves += mine
        steps[j] = mine
    pv = 0
    previous = {0: 0, 1: 0}
    for h in halves:
        h["pv_before"] = previous[h["slot"]]
        if h["kind"] == "P":
            pv += 1
            h["pv"] = pv
            previous[h["slot"]] = pv
    for u in units:
        mine = [h for h in halves if h["kind"] == "P" and units[h["u"]] is u]
        u["t_slot"], u["t_n"], u["pv"] = mine[-1]["slot"], mine[-1]["n"], mine[-1]["pv"]
    return nq, units, ring, steps, count, pv


def program(nc, x, bias1, cond, mask, g_in, null_bias, wq1, wkv1, wo1, g_out, wq2T, bq2, wk2T, bk2, wv2T,
            bv2, gamma, wtT, wgT, w_gate, w_up, w_down, sw_gate, sw_up, sw_down, w_router, w_block, out,
            kb0=None):
    top = ExitStack()
    with top:
        taken = []

        def once(name):
            taken.append(name)
            return f"{name}_{taken.count(name)}"

        def tensor(stack, name, shape, dt=F32):
            return stack.enter_context(nc.sbuf_tensor(once(name), shape, dt))

        def psum(stack, name, shape, dt=F32):
            return stack.enter_context(nc.psum_tensor(once(name), shape, dt))

        def sem(stack, name):
            return stack.enter_context(nc.semaphore(name))

        X = tensor(top, "X", [P, NT, D])
        FT = tensor(top, "FT", [P, KD, B * N])
        ident = tensor(top, "ident", [P, P])
        A = tensor(top, "A", [P, NT, D])
        stats = tensor(top, "stats", [P, NT, 6])
        mv = tensor(top, "mv", [P, NT, 2])
        rstd = tensor(top, "rstd", [P, NT])
        std = tensor(top, "std", [P, NT])
        half_v = tensor(top, "half_v", [P, NT])
        g_in_c = tensor(top, "g_in_c", [P, KD])
        g_out_b = tensor(top, "g_out_b", [P, D])

        def rstd_steps(dve, s_var, s_std, chain, after):
            after()
            dve.tensor_scalar(half_v[:, :], mv[:, :, 1], EPS, None, ALU.add).then_inc(s_var, 1)
            dve.wait_ge(s_std, 1)
            chain(dve.reciprocal(rstd[:, :], std[:, :]), True)
            chain(dve.tensor_tensor(std[:, :], rstd[:, :], rstd[:, :], ALU.mult), True)
            chain(dve.tensor_tensor(std[:, :], std[:, :], half_v[:, :], ALU.mult), True)
            chain(dve.tensor_scalar(std[:, :], std[:, :], -0.5, 1.5, ALU.mult, ALU.add), True)
            chain(dve.tensor_tensor(rstd[:, :], rstd[:, :], std[:, :], ALU.mult), True)

        def own_results(engine, own):
            count = [0]

            def after(newest=0):
                if count[0] > newest:
                    engine.wait_ge(own, count[0] - newest)

            def chain(instruction, wait=False):
                count[0] += 1
                instruction.then_inc(own, 1)
                if wait:
                    after()

            return chain, after, count

        with ExitStack() as s1:
            KT = tensor(s1, "KT", [G + 1, B * N])
            V1 = tensor(s1, "V1", [P, NT, DH])
            NSC = tensor(s1, "NSC", [P, H1, B, TB])
            nv_b = tensor(s1, "nv_b", [P, DH])
            Wo = tensor(s1, "Wo", [P, NP1, D])
            causal = tensor(s1, "causal", [P, P])
            OT = tensor(s1, "OT", [P, NP1, B * N])
            early_keys = tensor(s1, "early_keys", [G + 1, 1], mybir.dt.int32)

            with ExitStack() as st:
                Wkv = tensor(st, "Wkv", [P, KD, 2 * DH])
                Wq = tensor(st, "Wq", [P, KD, H1 * DH])
                Gn = tensor(st, "Gn", [P, KD, H1])
                prod = OT[:, 0, 0:KD * H1 * DH].rearrange("p (k h d) -> p k h d", k=KD, h=H1)
                nk_b = tensor(st, "nk_b", [P, DH])
                nb_b = tensor(st, "nb_b", [P, H1])
                mask_w = tensor(st, "mask_w", [G + 1, B * N // 4], mybir.dt.int32)
                xn = A
                s_x = sem(st, "s_x")
                s_w = sem(st, "s_w")
                s_small = sem(st, "s_small")
                s_dve = sem(st, "s_dve")
                s_id = sem(st, "s_id")
                s_var = sem(st, "s_var")
                s_std = sem(st, "s_std")
                s_xn = sem(st, "s_xn")
                s_tr = sem(st, "s_tr")
                s_ft = sem(st, "s_ft")
                s_k = sem(st, "s_k")
                s_v = sem(st, "s_v")
                s_ns = sem(st, "s_ns")
                s_prod = sem(st, "s_prod")
                seen = tensor(st, "seen", [G + 1, 1])
                s_gn = sem(st, "s_gn")
                s_kcopy = sem(st, "s_kcopy")
                psT = [psum(st, f"psT{i}", [P, CH]) for i in range(2)]
                psK = [psum(st, f"psK{i}", [P, CH]) for i in range(2)]
                psV = psum(st, "psV", [P, 2, CH])
                psN = psum(st, "psN", [P, NT, H1])
                blk = st.enter_context(nc.Block())

                @blk.sync
                def _(sp):
                    xv = x.rearrange("b (t p) d -> p (b t) d", p=P)
                    for c in range(4):
                        sp.dma_start(X[:, 4 * c:4 * c + 4, :], xv[:, 4 * c:4 * c + 4, :]).then_inc(s_x, 16)
                    sp.dma_start(Wkv[:, :, :], wkv1.rearrange("(k p) n -> p k n", p=P)).then_inc(s_w, 16)
                    sp.dma_start(Wq[:, :, :], wq1.rearrange("(k p) n -> p k n", p=P)).then_inc(s_w, 16)
                    sp.dma_start(Wo[:, :, :], wo1.rearrange("(k p) n -> p k n", p=P)).then_inc(s_w, 16)
                    sp.wait_ge(s_w, 48)

                @blk.scalar
                def _(act):
                    small = [(nk_b[:, :], cond[0:1, :].broadcast_to([P, G])),
                             (nv_b[:, :], cond[1:2, :].broadcast_to([P, G])),
                             (nb_b[:, :], null_bias.rearrange("(a h) -> a h", a=1).broadcast_to([P, H1])),
                             (g_out_b[:, :], g_out.rearrange("(a h) -> a h", a=1).broadcast_to([P, D])),
                             (mask_w[G:G + 1, :], mask.rearrange("b n -> (b n)").rearrange("(a n) -> a n", a=1))]
                    for to, src in small:
                        act.dma_start(to, src).then_inc(s_small, 16)
                    for k in range(KD):
                        act.dma_start(g_in_c[:, k:k + 1], g_in[k * P:(k + 1) * P].rearrange("(p a) -> p a", a=1)
                                      ).then_inc(s_small, 16)
                    act.wait_ge(s_var, 1)
                    act.activation(std[:, :], half_v[:, :], ACT.Sqrt).then_inc(s_std, 1)
                    act.wait_ge(s_small, 16 * (len(small) + KD))
                    for c in range(NC_):
                        for k in range(KD):
                            n = c * KD + k
                            act.wait_ge(s_tr, n + 1)
                            act.activation(FT[:, k, c * CH:(c + 1) * CH], psT[n % 2][:, :], ACT.Copy,
                                           scale=g_in_c[:, k:k + 1]).then_inc(s_ft, 1)

                @blk.gpsimd
                def _(pool):
                    pool.memset(ident[:, :], 0.0).then_inc(s_id, 1)
                    pool.wait_ge(s_id, 1)
                    pool.affine_select(out=ident[:, :], in_=ident[:, :], compare_op=ALU.not_equal, fill=1.0,
                                       base=0, pattern=[[-1, P]], channel_multiplier=1).then_inc(s_id, 1)
                    pool.memset(causal[:, :], 0.0).then_inc(s_id, 1)
                    pool.wait_ge(s_id, 3)
                    pool.affine_select(out=causal[:, :], in_=causal[:, :], compare_op=ALU.is_ge, fill=NEG,
                                       base=0, pattern=[[-1, P]], channel_multiplier=1).then_inc(s_id, 1)
                    pool.wait_ge(s_w, 48)
                    pool.wait_ge(s_small, 16 * 7)
                    for k in range(KD):
                        pool.tensor_tensor(prod[:, k], Wq[:, k, :].rearrange("p (h d) -> p h d", h=H1),
                                           nk_b[:, :].unsqueeze(1).broadcast_to([P, H1, DH]), ALU.mult
                                           ).then_inc(s_prod, 1)

                @blk.vector
                def _(dve):
                    chain, after, count = own_results(dve, s_dve)
                    dve.wait_ge(s_x, 16 * (NT // 4))
                    for t in range(NT):
                        chain(dve.bn_stats(stats[:, t, :], X[:, t, :]))
                    after()
                    for t in range(NT):
                        chain(dve.bn_aggr(mv[:, t, :], stats[:, t, :]))
                    rstd_steps(dve, s_var, s_std, chain, after)
                    for t in range(NT):
                        dve.tensor_scalar(xn[:, t, :], X[:, t, :], mv[:, t, 0:1], rstd[:, t:t + 1],
                                          ALU.subtract, ALU.mult).then_inc(s_xn, 1)
                    dve.wait_ge(s_prod, KD)
                    dve.tensor_reduce(Gn[:, :, :], prod, AX_X, ALU.add).then_inc(s_gn, 1)
                    dve.wait_ge(s_small, 16 * 7)
                    chain(dve.tensor_scalar(KT[G:G + 1, :], mask_w[G:G + 1, :].bitcast(U8), 1.0, -NEG, ALU.subtract, ALU.mult))
                    chain(dve.tensor_scalar(nb_b[:, :], nb_b[:, :], -1.0, None, ALU.mult))
                    after()
                    chain(dve.tensor_reduce(seen[G:G + 1, :], KT[G:G + 1, :].rearrange("p (b n) -> p b n", b=B)
                                            [:, :, 0:(TB - 2) * P], mybir.AxisListType.XY, ALU.max), True)
                    chain(dve.tensor_scalar(early_keys[G:G + 1, :], seen[G:G + 1, :], 0.5 * NEG, None, ALU.is_ge))
                    for c in range(NC_):
                        dve.wait_ge(s_k, c + 1)
                        dve.tensor_copy(KT[0:G, c * CH:(c + 1) * CH], psK[c % 2][0:G, :]).then_inc(s_kcopy, 1)
                    for c in range(2):
                        dve.wait_ge(s_v, c + 1)
                        chain(dve.tensor_copy(V1[:, c * TB:(c + 1) * TB, :],
                                              psV[:, c, :].rearrange("p (t d) -> p t d", d=DH)))
                    dve.wait_ge(s_ns, 1)
                    for b in range(B):
                        chain(dve.scalar_tensor_tensor(
                            out=NSC[:, :, b, :].rearrange("p h t -> p t h"), in0=psN[:, b * TB:(b + 1) * TB, :],
                            scalar=-float(DH) ** -0.5, in1=nb_b[:, :].unsqueeze(1).broadcast_to([P, TB, H1]),
                            op0=ALU.mult, op1=ALU.add))

                @blk.tensor
                def _(pe):
                    pe.wait_ge(s_id, 2)
                    for c in range(NC_):
                        for k in range(KD):
                            n = c * KD + k
                            pe.wait_ge(s_xn, 4 * c + 4)
                            if n >= 2:
                                pe.wait_ge(s_ft, n - 1)
                            for t in range(4):
                                mm = pe.transpose(psT[n % 2][:, t * P:(t + 1) * P],
                                                  xn[:, 4 * c + t, k * P:(k + 1) * P], ident[:, :])
                            mm.then_inc(s_tr, 1)
                    pe.wait_ge(s_ft, NC_ * KD)
                    pe.wait_ge(s_w, 48)
                    for c in range(NC_):
                        if c >= 2:
                            pe.wait_ge(s_kcopy, c - 1)
                        for k in range(KD):
                            mm = pe.matmul(psK[c % 2][0:DH, :], Wkv[:, k, 0:DH], FT[:, k, c * CH:(c + 1) * CH],
                                           start=k == 0, stop=k == KD - 1)
                        mm.then_inc(s_k, 1)
                    for t in range(NT):
                        for k in range(KD):
                            mm = pe.matmul(psV[:, t // TB, (t % TB) * DH:(t % TB + 1) * DH],
                                           FT[:, k, t * P:(t + 1) * P], Wkv[:, k, DH:2 * DH],
                                           start=k == 0, stop=k == KD - 1)
                        if t % TB == TB - 1:
                            mm.then_inc(s_v, 1)
                    pe.wait_ge(s_gn, 1)
                    for t in range(NT):
                        for k in range(KD):
                            mm = pe.matmul(psN[:, t, :], FT[:, k, t * P:(t + 1) * P], Gn[:, k, :],
                                           start=k == 0, stop=k == KD - 1)
                    mm.then_inc(s_ns, 1)


            def attend(kb0):
                UNR = 2 if kb0 >= TB // 2 else 1
                nq, units, ring, steps, per_slot, per_pv = half_plan(kb0, UNR)
                NQ = nq * P
                NU = len(units)
                NR = len(ring)
                NBIAS = NU // B
                NG = 2 * UNR
                NBR = 4
                WMAX = NQ
                q_at = {(it[1], it[2]): n for n, it in enumerate(ring) if it[0] == "q"}
                CR = {"ring": NR, "t": max(per_slot), "evac": 2, "pv": per_pv}
                with ExitStack() as st:
                    Wqs = [tensor(st, f"Wqs{s}", [P, KD, P]) for s in range(UNR)]
                    qT = [[tensor(st, f"qT{s}{he}", [G + 1, B, NQ]) for he in range(2)] for s in range(UNR)]
                    NSs = [tensor(st, f"NSs{s}", [P, 2, B, TB]) for s in range(UNR)]
                    BI = [tensor(st, f"BI{i}", [P, WMAX]) for i in range(NBR)]
                    SS = [tensor(st, f"SS{i}", [P, WMAX]) for i in range(2)]
                    PT = [tensor(st, f"PT{i}", [P, 4, P]) for i in range(2)]
                    nm = tensor(st, "nm", [P, NG, B, nq])
                    rs = tensor(st, "rs", [P, NG, B, nq])
                    darg = tensor(st, "darg", [P, NG, B, nq])
                    en = tensor(st, "en", [P, NG, B, nq])
                    tmp = [tensor(st, f"tmp{b}", [P, nq, DH]) for b in range(B)]
                    ON = [tensor(st, f"ON{s}", [P, B, nq, 2 * DH]) for s in range(UNR)]
                    psS = [psum(st, f"psS{i}", [P, 2 * CH]) for i in range(2)]
                    psT = [psum(st, f"psTt{i}", [P, 4, P]) for i in range(2)]
                    psO = [psum(st, f"psO{b}", [P, TB, DH]) for b in range(B)]
                    s_wq = [sem(st, f"s_wq{s}") for s in range(UNR)]
                    bias_loaded = [sem(st, f"bias_loaded{i}") for i in range(NBR)]
                    bias_ready = sem(st, "bias_ready")
                    null_staged = sem(st, "null_staged")
                    s_done = sem(st, "s_done")
                    ring_free = sem(st, "ring_free")
                    exp_done = sem(st, "exp_done")
                    t_done = [sem(st, f"t_done{i}") for i in range(2)]
                    evac_done = [sem(st, f"evac_done{i}") for i in range(2)]
                    pv_done = sem(st, "pv_done")
                    darg_done = sem(st, "darg_done")
                    en_done = sem(st, "en_done")
                    tmp_done = sem(st, "tmp_done")
                    l_done = sem(st, "l_done")
                    r_done = sem(st, "r_done")
                    o1_done = sem(st, "o1_done")
                    fin_done = sem(st, "fin_done")
                    ones_done = sem(st, "ones_done")
                    blk = st.enter_context(nc.Block())
                    LOOPS = NP1 // UNR

                    def width(u):
                        return (u["qt"] + 1 - kb0) * P

                    @blk.sync
                    def _(sp):
                        with sp.Fori(0, LOOPS) as i:
                            for s in range(UNR):
                                sp.wait_ge(s_done, i * NR + q_at[(s, B - 1)] + 1)
                                for k in range(KD):
                                    sp.dma_start(Wqs[s][:, k, :], wq1[k * P:(k + 1) * P, bass.ds((i * UNR + s) * P, P)]
                                                 ).then_inc(s_wq[s], 16)
                            for bu in range(NBIAS):
                                u = units[bu * B]
                                back = units[(bu - NBR) * B + 1]["ring"] + 1 - (NR if bu < NBR else 0)
                                sp.wait_ge(ring_free, i * NR + back + CR["ring"])
                                head = (i * UNR + u["s"]) * 2 + u["he"]
                                sp.dma_start(BI[bu % NBR][:, 0:width(u)],
                                             bias1[bass.ds(head, 1), u["qt"] * P:(u["qt"] + 1) * P,
                                                   kb0 * P:(u["qt"] + 1) * P].rearrange("a p n -> p (a n)")
                                             ).then_inc(bias_loaded[bu % NBR], 16)

                    @blk.gpsimd
                    def _(pool):
                        with pool.Fori(0, LOOPS) as i:
                            for j in range(-2, NU + 5):
                                for bu in range(NBIAS):
                                    if bu * B == j + 2:
                                        u = units[bu * B]
                                        pool.wait_ge(bias_loaded[bu % NBR],
                                                     (i * (NBIAS // NBR) + bu // NBR + 1) * 16)
                                        diag = BI[bu % NBR][:, width(u) - P:width(u)]
                                        pool.tensor_tensor(diag, diag, causal[:, :], ALU.add).then_inc(bias_ready, 1)
                                e = j - 2
                                if 0 <= e < NU and units[e]["last"] and units[e]["b"] == B - 1:
                                    g = units[e]["g"]
                                    pool.wait_ge(en_done, i * NG + g + 1)
                                    pool.wait_ge(fin_done, i * NG + g + NG)
                                    for b in range(B):
                                        pool.tensor_tensor(tmp[b][:, :, :],
                                                           nv_b[:, :].unsqueeze(1).broadcast_to([P, nq, DH]),
                                                           en[:, g, b, :].unsqueeze(2).broadcast_to([P, nq, DH]),
                                                           ALU.mult).then_inc(tmp_done, 1)

                    @blk.tensor
                    def _(pe):
                        pe.sem_inc(s_done, NR)
                        for i2 in range(2):
                            pe.sem_inc(t_done[i2], CR["t"])
                        pe.sem_inc(pv_done, CR["pv"])
                        pe.wait_ge(ones_done, 2 * UNR)
                        with pe.Fori(0, LOOPS) as i:
                            at = 0
                            for j in range(-2, NU + 5):
                                for h in steps[j]:
                                    if h["kind"] == "P":
                                        if h["first"]:
                                            pe.wait_ge(exp_done, i * NU + h["u"] + 1)
                                        pe.wait_ge(evac_done[h["slot"]], i * per_slot[h["slot"]] + h["n"] - 1 + CR["evac"])
                                        for c, kb in enumerate(h["blocks"]):
                                            mm = pe.transpose(psT[h["slot"]][:, c, :],
                                                              SS[h["u"] % 2][:, (kb - kb0) * P:(kb - kb0 + 1) * P],
                                                              ident[:, :])
                                        mm.then_inc(t_done[h["slot"]], 1)
                                if j + 2 < NU:
                                    while at <= units[j + 2]["ring"]:
                                        item = ring[at]
                                        if item[0] == "q":
                                            _, s, b = item
                                            pe.wait_ge(s_wq[s], (i + 1) * 16 * KD)
                                            pe.wait_ge(ring_free, i * NR + at - 1 + CR["ring"])
                                            for c0 in range(0, NQ, CH):
                                                w = min(CH, NQ - c0)
                                                for k in range(KD):
                                                    mm = pe.matmul(psS[at % 2][:, c0:c0 + w], Wqs[s][:, k, :],
                                                                   FT[:, k, b * N + kb0 * P + c0:b * N + kb0 * P + c0 + w],
                                                                   start=k == 0, stop=k == KD - 1)
                                        else:
                                            u = units[item[1]]
                                            pe.wait_ge(ring_free, i * NR + max(at - 1, q_at[(u["s"], u["b"])] + 1)
                                                       + CR["ring"])
                                            q0 = (u["qt"] - kb0) * P
                                            for c0 in range(0, width(u), CH):
                                                w = min(CH, width(u) - c0)
                                                k0 = u["b"] * N + kb0 * P + c0
                                                mm = pe.matmul(psS[at % 2][:, c0:c0 + w],
                                                               qT[u["s"]][u["he"]][:, u["b"], q0:q0 + P],
                                                               KT[:, k0:k0 + w], start=True, stop=True)
                                        mm.then_inc(s_done, 1)
                                        at += 1
                                if 0 <= j - 1 < NU:
                                    u = units[j - 1]
                                    if u["first"] and u["b"] == 0:
                                        pe.wait_ge(o1_done, (i * NG + u["g"]) * B + 2)
                                    for h in steps[j - 1]:
                                        if h["kind"] != "P":
                                            continue
                                        pe.wait_ge(evac_done[h["slot"]], i * per_slot[h["slot"]] + h["n"] + CR["evac"])
                                        for c, kb in enumerate(h["blocks"]):
                                            mm = pe.matmul(psO[u["b"]][:, u["qt"] - kb0, :], PT[h["slot"]][:, c, :],
                                                           V1[:, u["b"] * TB + kb, :], start=kb == kb0,
                                                           stop=kb == u["qt"])
                                        mm.then_inc(pv_done, 1)
                                for h in steps[j]:
                                    if h["kind"] == "O":
                                        pe.wait_ge(fin_done, i * NG + h["g"] + 1 + NG)
                                        pe.wait_ge(evac_done[h["slot"]], i * per_slot[h["slot"]] + h["n"] - 1 + CR["evac"])
                                        for c, (b, qt) in enumerate(h["tiles"]):
                                            mm = pe.transpose(psT[h["slot"]][:, c, :], ON[h["s"]][:, b, qt - kb0, :], ident[:, :])
                                        mm.then_inc(t_done[h["slot"]], 1)

                    def copy_out(eng, i, h, copy):
                        eng.wait_ge(t_done[h["slot"]], i * per_slot[h["slot"]] + h["n"] + CR["t"])
                        if h["kind"] == "P":
                            eng.wait_ge(pv_done, i * per_pv + h["pv_before"] + CR["pv"])
                            n = len(h["blocks"])
                            copy(PT[h["slot"]][:, 0:n, :], psT[h["slot"]][:, 0:n, :]).then_inc(evac_done[h["slot"]], 1)
                        else:
                            tiles, c = h["tiles"], 0
                            while c < len(tiles):
                                e = c
                                while e + 1 < len(tiles) and tiles[e + 1][0] == tiles[c][0]:
                                    e += 1
                                b, qt = tiles[c]
                                n = e + 1 - c
                                ins = copy(OT[:, bass.ds(i * UNR + h["s"], 1), b * N + qt * P:b * N + (qt + n) * P]
                                           .rearrange("p a n -> p (a n)"),
                                           psT[h["slot"]][:, c:c + n, :].rearrange("p a n -> p (a n)"))
                                c = e + 1
                            ins.then_inc(evac_done[h["slot"]], 1)

                    @blk.scalar
                    def _(act):
                        act.sem_inc(evac_done[0], CR["evac"])
                        with act.Fori(0, LOOPS) as i:
                            for s in range(UNR):
                                act.wait_ge(fin_done, i * NG + 2 * s + 2)
                                act.copy(NSs[s][:, :, :, :], NSC[:, bass.ds((i * UNR + s) * 2, 2), :, :]
                                         ).then_inc(null_staged, 1)
                            for j in range(-2, NU + 5):
                                if 0 <= j + 1 < NU:
                                    u = units[j + 1]
                                    act.wait_ge(ring_free, i * NR + u["ring"] + 1 + CR["ring"])
                                    S = SS[(j + 1) % 2][:, 0:width(u)]
                                    act.activation(S, S, ACT.Exp, scale=-1.0,
                                                   bias=nm[:, u["g"], u["b"], u["qt"] - kb0:u["qt"] - kb0 + 1],
                                                   accum_out=rs[:, u["g"], u["b"], u["qt"] - kb0:u["qt"] - kb0 + 1]
                                                   ).then_inc(exp_done, 1)
                                e = j - 1
                                if 0 <= e < NU and units[e]["last"] and units[e]["b"] == B - 1:
                                    g = units[e]["g"]
                                    act.wait_ge(darg_done, i * NG + g + 1)
                                    act.activation(en[:, g, :, :], darg[:, g, :, :], ACT.Exp).then_inc(en_done, 1)
                                for h in steps[j]:
                                    if h["slot"] == 0:
                                        copy_out(act, i, h, act.copy)

                    @blk.vector
                    def _(dve):
                        for s in range(UNR):
                            for he in range(2):
                                dve.memset(qT[s][he][G:G + 1, :, :], 1.0).then_inc(ones_done, 1)
                        dve.sem_inc(evac_done[1], CR["evac"])
                        dve.sem_inc(ring_free, CR["ring"])
                        dve.sem_inc(fin_done, NG)
                        dve.sem_inc(o1_done, B)
                        with dve.Fori(0, LOOPS) as i:
                            at = 0
                            for j in range(-2, NU + 5):
                                if j + 1 < NU and j >= -1:
                                    while at <= units[j + 1]["ring"]:
                                        item = ring[at]
                                        dve.wait_ge(s_done, i * NR + at + 1 + NR)
                                        if item[0] == "q":
                                            _, s, b = item
                                            for he in range(2):
                                                ins = dve.tensor_scalar(qT[s][he][0:DH, b, :],
                                                                        psS[at % 2][he * DH:(he + 1) * DH, 0:NQ],
                                                                        float(DH) ** -0.5, None, ALU.mult)
                                        else:
                                            n = item[1]
                                            u = units[n]
                                            w = width(u)
                                            ql = u["qt"] - kb0
                                            dve.wait_ge(bias_ready, i * NBIAS + n // B + 1)
                                            dve.wait_ge(null_staged, i * UNR + u["s"] + 1)
                                            if n >= 2:
                                                v = units[n - 2]
                                                dve.wait_ge(t_done[v["t_slot"]],
                                                            i * per_slot[v["t_slot"]] + v["t_n"] + CR["t"])
                                            else:
                                                v = units[NU - 2 + n]
                                                dve.wait_ge(t_done[v["t_slot"]],
                                                            i * per_slot[v["t_slot"]] + v["t_n"] - per_slot[v["t_slot"]]
                                                            + CR["t"])
                                            ins = dve.tensor_tensor_reduce(
                                                out=SS[n % 2][:, 0:w], in0=psS[at % 2][:, 0:w], in1=BI[(n // B) % NBR][:, 0:w],
                                                scale=-1.0, scalar=NSs[u["s"]][:, u["he"], u["b"], u["qt"]:u["qt"] + 1],
                                                op0=ALU.add, op1=ALU.min,
                                                accum_out=nm[:, u["g"], u["b"], ql:ql + 1])
                                            ins.wait_op(ring_free, 1, "sem-ge")
                                        ins.then_inc(ring_free, 1)
                                        at += 1
                                e = j
                                if 0 <= e < NU and units[e]["last"] and units[e]["b"] == B - 1:
                                    g, s, he = units[e]["g"], units[e]["s"], units[e]["he"]
                                    dve.wait_ge(ring_free, i * NR + units[e]["ring"] + 1 + CR["ring"])
                                    dve.tensor_tensor(darg[:, g, :, :], nm[:, g, :, :], NSs[s][:, he, :, kb0:TB],
                                                      ALU.subtract).then_inc(darg_done, 1)
                                e = j - 2
                                if 0 <= e < NU and units[e]["last"] and units[e]["b"] == B - 1:
                                    u = units[e]
                                    g, s, he = u["g"], u["s"], u["he"]
                                    dve.wait_ge(exp_done, i * NU + e + 1)
                                    dve.wait_ge(en_done, i * NG + g + 1)
                                    dve.tensor_tensor(rs[:, g, :, :], rs[:, g, :, :], en[:, g, :, :], ALU.add
                                                      ).then_inc(l_done, 1)
                                    dve.wait_ge(l_done, i * NG + g + 1)
                                    dve.reciprocal(rs[:, g, :, :], rs[:, g, :, :]).then_inc(r_done, 1)
                                    dve.wait_ge(pv_done, i * per_pv + u["pv"] + CR["pv"])
                                    dve.wait_ge(tmp_done, (i * NG + g + 1) * B)
                                    for b in range(B):
                                        dve.tensor_tensor(tmp[b][:, :, :], psO[b][:, 0:nq, :], tmp[b][:, :, :], ALU.add
                                                          ).then_inc(o1_done, 1)
                                    dve.wait_ge(o1_done, (i * NG + g + 1) * B + 2)
                                    dve.wait_ge(r_done, i * NG + g + 1)
                                    if he == 0:
                                        v = [h for js in steps.values() for h in js if h["kind"] == "O" and h["s"] == s][-1]
                                        dve.wait_ge(t_done[v["slot"]], i * per_slot[v["slot"]] + v["n"]
                                                    - per_slot[v["slot"]] + CR["t"])
                                    for b in range(B):
                                        ins = dve.tensor_tensor(ON[s][:, b, :, he * DH:(he + 1) * DH], tmp[b][:, :, :],
                                                                rs[:, g, b, :].unsqueeze(2).broadcast_to([P, nq, DH]),
                                                                ALU.mult)
                                    ins.then_inc(fin_done, 1)
                                for h in steps[j]:
                                    if h["slot"] == 1:
                                        copy_out(dve, i, h, dve.tensor_copy)


                with ExitStack() as st:
                    y0 = tensor(st, "y0", [P, D])
                    tiles = [b * TB + qt for b in range(B) for qt in range(kb0, TB)]
                    nvT = tensor(st, "nvT", [P, P])
                    nv_c = tensor(st, "nv_c", [P, 1])
                    s_nv = sem(st, "s_nv")
                    s_nvT = sem(st, "s_nvT")
                    s_y = sem(st, "s_y")
                    s_e = sem(st, "s_e")
                    s_dve = sem(st, "s_dve")
                    s_var = sem(st, "s_var")
                    s_std = sem(st, "s_std")
                    s_n = sem(st, "s_n")
                    s_a = sem(st, "s_a")
                    psY = [psum(st, f"psY{i}", [P, CH]) for i in range(4)]
                    blk = st.enter_context(nc.Block())
                    todo = tiles + ([0] if kb0 else [])
                    same = [b * TB + qt for b in range(B) for qt in range(kb0)][1:]

                    @blk.sync
                    def _(sp):
                        for c in range(2):
                            sp.dma_start(nv_c[c * DH:(c + 1) * DH, :], cond[1:2, :].rearrange("a d -> d a")).then_inc(s_nv, 16)
                        sp.wait_ge(s_nv, 32)

                    @blk.tensor
                    def _(pe):
                        for n, t in enumerate(todo):
                            if n >= 4:
                                pe.wait_ge(s_e, n - 3)
                            null = n >= len(tiles)
                            if null:
                                pe.wait_ge(s_nvT, 1)
                            for k in range(NP1):
                                w = nvT[:, :] if null else OT[:, k, t * P:(t + 1) * P]
                                mm = pe.matmul(psY[n % 4][:, 0:D], w, Wo[:, k, :], start=k == 0, stop=k == NP1 - 1)
                            mm.then_inc(s_y, 1)

                    @blk.scalar
                    def _(act):
                        for n, t in enumerate(todo):
                            act.wait_ge(s_y, n + 1)
                            act.copy(A[:, t, :], psY[n % 4][:, 0:D]).then_inc(s_e, 1)
                        act.wait_ge(s_var, 1)
                        act.activation(std[:, :], half_v[:, :], ACT.Sqrt).then_inc(s_std, 1)
                        if kb0:
                            act.wait_ge(s_a, len(todo))
                            for t in same:
                                act.copy(A[:, t, :], A[:, 0, :])

                    @blk.gpsimd
                    def _(pool):
                        for n, t in enumerate(todo):
                            pool.wait_ge(s_n, n + 1)
                            pool.tensor_tensor(A[:, t, :], A[:, t, :], g_out_b[:, :], ALU.mult).then_inc(s_a, 1)

                    @blk.vector
                    def _(dve):
                        chain, after, count = own_results(dve, s_dve)
                        dve.wait_ge(s_nv, 32)
                        dve.tensor_copy(nvT[:, :], nv_c[:, 0:1].broadcast_to([P, P])).then_inc(s_nvT, 1)
                        for n, t in enumerate(todo):
                            dve.wait_ge(s_e, n + 1)
                            chain(dve.bn_stats(stats[:, t, :], A[:, t, :]))
                        after()
                        for t in todo:
                            chain(dve.bn_aggr(mv[:, t, :], stats[:, t, :]))
                        rstd_steps(dve, s_var, s_std, chain, after)
                        for t in todo:
                            dve.tensor_scalar(A[:, t, :], A[:, t, :], mv[:, t, 0:1], rstd[:, t:t + 1],
                                              ALU.subtract, ALU.mult).then_inc(s_n, 1)

            if kb0 is None:
                early = nc.values_load(early_keys[G:G + 1, 0:1], min_val=0, max_val=1)
                with nc.If(early == 0):
                    attend(TB - 2)
                with nc.Else():
                    attend(0)
            else:
                attend(kb0)


        X1 = tensor(top, "X1", [P, NT, D])
        with ExitStack() as s2:
            V2 = tensor(s2, "V2", [P, NT, H2 * DV])
            OB = tensor(s2, "OB", [P, NT, H2 * DV])
            parts_dram = [nc.dram_tensor(f"parts_{n}", (3, H2 * DQ, B * N), BF16).ap() for n in "qk"]
            with ExitStack() as st:
                W2 = [tensor(st, f"W2{n}", [P, KD, H2 * DQ]) for n in "qk"]
                b2 = [tensor(st, f"b2{n}", [H2 * DQ, 1]) for n in "qk"]
                Wv = tensor(st, "Wv", [P, KD, D])
                bv_b = tensor(st, "bv_b", [P, D])
                QF = [tensor(st, f"QF{n}", [H2 * DQ, B * N]) for n in "qk"]
                RF = tensor(st, "RF", [H2 * DQ, B * N])
                PA = [tensor(st, f"PA{n}", [H2 * DQ, 3, B * N], BF16) for n in "qk"]
                s_w = sem(st, "s_w")
                s_tr = sem(st, "s_tr")
                s_ft = sem(st, "s_ft")
                s_q = sem(st, "s_q")
                s_qf = sem(st, "s_qf")
                s_v = sem(st, "s_v")
                s_vc = sem(st, "s_vc")
                s_dve = sem(st, "s_dve")
                s_parts = [sem(st, f"s_parts{n}") for n in "qk"]
                s_out = sem(st, "s_out")
                psT = [psum(st, f"psT{i}", [P, CH]) for i in range(2)]
                psQ = [psum(st, f"psQ{i}", [P, CH]) for i in range(2)]
                psV = [psum(st, f"psV{i}", [P, CH]) for i in range(2)]
                blk = st.enter_context(nc.Block())

                @blk.sync
                def _(sp):
                    for n, (w, bb) in enumerate(((wq2T, bq2), (wk2T, bk2))):
                        sp.dma_start(W2[n][:, :, :], w.rearrange("(k p) n -> p k n", p=P)).then_inc(s_w, 16)
                        sp.dma_start(b2[n][:, :], bb.rearrange("(p a) -> p a", a=1)).then_inc(s_w, 16)
                    sp.dma_start(Wv[:, :, :], wv2T.rearrange("(k p) n -> p k n", p=P)).then_inc(s_w, 16)
                    sp.dma_start(bv_b[:, :], bv2.rearrange("(a n) -> a n", a=1).broadcast_to([P, D])).then_inc(s_w, 16)
                    for n in range(2):
                        sp.wait_ge(s_parts[n], 1)
                        sp.dma_start(parts_dram[n].rearrange("a p n -> p a n"), PA[n][:, :, :]).then_inc(s_out, 16)
                    sp.wait_ge(s_out, 32)

                @blk.tensor
                def _(pe):
                    for c in range(NC_):
                        for k in range(KD):
                            n = c * KD + k
                            if n >= 2:
                                pe.wait_ge(s_ft, n - 1)
                            for t in range(4):
                                mm = pe.transpose(psT[n % 2][:, t * P:(t + 1) * P],
                                                  A[:, 4 * c + t, k * P:(k + 1) * P], ident[:, :])
                            mm.then_inc(s_tr, 1)
                    pe.wait_ge(s_ft, NC_ * KD)
                    pe.wait_ge(s_w, 96)
                    for n in range(2):
                        for c in range(NC_):
                            m = n * NC_ + c
                            if m >= 2:
                                pe.wait_ge(s_qf, m - 1)
                            for k in range(KD):
                                mm = pe.matmul(psQ[m % 2][0:H2 * DQ, :], W2[n][:, k, :], FT[:, k, c * CH:(c + 1) * CH],
                                               start=k == 0, stop=k == KD - 1)
                            mm.then_inc(s_q, 1)
                    for t in range(NT):
                        if t >= 2:
                            pe.wait_ge(s_vc, t - 1)
                        for k in range(KD):
                            mm = pe.matmul(psV[t % 2][:, 0:D], FT[:, k, t * P:(t + 1) * P], Wv[:, k, :],
                                           start=k == 0, stop=k == KD - 1)
                        mm.then_inc(s_v, 1)

                @blk.scalar
                def _(act):
                    for c in range(NC_):
                        for k in range(KD):
                            n = c * KD + k
                            act.wait_ge(s_tr, n + 1)
                            act.copy(FT[:, k, c * CH:(c + 1) * CH], psT[n % 2][:, :]).then_inc(s_ft, 1)

                @blk.vector
                def _(dve):
                    chain, after, count = own_results(dve, s_dve)
                    dve.wait_ge(s_w, 96)
                    for n in range(2):
                        for c in range(NC_):
                            dve.wait_ge(s_q, n * NC_ + c + 1)
                            dve.tensor_scalar(QF[n][:, c * CH:(c + 1) * CH], psQ[(n * NC_ + c) % 2][0:H2 * DQ, :],
                                              b2[n][:, 0:1], float(DQ) ** -0.5 if n == 0 else 1.0,
                                              ALU.add, ALU.mult).then_inc(s_qf, 1)
                        dve.wait_ge(s_qf, (n + 1) * NC_)
                        rest = QF[n]
                        for a in range(3):
                            ins = dve.tensor_copy(PA[n][:, a, :], rest[:, :])
                            if a == 2:
                                ins.then_inc(s_parts[n], 1)
                            else:
                                chain(ins, True)
                                chain(dve.tensor_tensor(RF[:, :], rest[:, :], PA[n][:, a, :], ALU.subtract), True)
                                rest = RF
                    for t in range(NT):
                        dve.wait_ge(s_v, t + 1)
                        dve.tensor_tensor(V2[:, t, :], psV[t % 2][:, 0:D], bv_b[:, :], ALU.add).then_inc(s_vc, 1)

            with ExitStack() as st:
                NU = B * TB
                GU = 4
                NG = NU // GU
                PAIRS = [(3, 0), (2, 1), (1, 2)]
                KS = DQ * 6
                QA = [tensor(st, f"QA{b}", [KS, N], BF16) for b in range(B)]
                KA = [tensor(st, f"KA{b}", [KS, N], BF16) for b in range(B)]
                VA = [tensor(st, f"VA{b}", [P, TB, DV + 1]) for b in range(B)]
                RA = [tensor(st, f"RA{i}", [P, N]) for i in range(2)]
                UU = [tensor(st, f"UU{i}", [P, N]) for i in range(2)]
                nm = [tensor(st, f"nm{i}", [P, 1]) for i in range(2)]
                PT = [tensor(st, f"PT{i}", [P, TB, GU, P]) for i in range(2)]
                OS = [tensor(st, f"OS{i}", [DV + 1, GU, P]) for i in range(2)]
                rl = [tensor(st, f"rl{i}", [P, GU]) for i in range(2)]
                psS = [psum(st, f"psS{i}", [P, N]) for i in range(2)]
                psT = [psum(st, f"psTt{i}", [P, 4, P]) for i in range(2)]
                psO = [psum(st, f"psO{i}", [P, GU, P]) for i in range(2)]
                qk_loaded = [sem(st, f"qk_loaded{b}") for b in range(B)]
                ones_done = sem(st, "ones_done")
                va_done = sem(st, "va_done")
                s_done = sem(st, "s_done")
                relu_done = sem(st, "relu_done")
                ttr_done = sem(st, "ttr_done")
                exp_done = sem(st, "exp_done")
                t_done = sem(st, "t_done")
                evac_done = sem(st, "evac_done")
                pv_done = sem(st, "pv_done")
                os_done = sem(st, "os_done")
                ot_done = sem(st, "ot_done")
                rl_done = sem(st, "rl_done")
                out_done = sem(st, "out_done")
                blk = st.enter_context(nc.Block())

                def wait(eng, signal, value):
                    if not isinstance(value, int) or value > 0:
                        eng.wait_ge(signal, value)

                def passes(eng, steps):
                    steps(0, -2, NU)
                    with eng.Fori(1, H2 - 1) as i:
                        steps(i, 0, NU)
                    steps(H2 - 1, 0, NU + GU + 2)

                def unit_at(i, j):
                    if j < 0:
                        return (i - 1, j + NU) if not isinstance(i, int) or i > 0 else None
                    if j >= NU:
                        return (i + 1, j - NU) if not isinstance(i, int) or i < H2 - 1 else None
                    return i, j

                def group_end(at):
                    return at is not None and at[1] % GU == GU - 1

                @blk.sync
                def _(sp):
                    def load(i):
                        for b in range(B):
                            wait(sp, s_done, (i - 1) * NU + (b + 1) * TB)
                            row = 0
                            for n, first in PAIRS:
                                sp.dma_start(QA[b][row:row + n * DQ, :],
                                             parts_dram[0][0:n, bass.ds(i * DQ, DQ), b * N:(b + 1) * N]
                                             ).then_inc(qk_loaded[b], 16)
                                for c in range(n):
                                    sp.dma_start(KA[b][row + c * DQ:row + (c + 1) * DQ, :],
                                                 parts_dram[1][first, bass.ds(i * DQ, DQ), b * N:(b + 1) * N]
                                                 ).then_inc(qk_loaded[b], 16)
                                row += n * DQ
                    load(0)
                    with sp.Fori(1, H2) as i:
                        load(i)

                LOADS = 16 * (len(PAIRS) + 6)

                @blk.gpsimd
                def _(pool):
                    for b in range(B):
                        pool.memset(VA[b][:, :, DV:DV + 1], 1.0).then_inc(ones_done, 1)

                @blk.tensor
                def _(pe):
                    pe.wait_ge(ones_done, B)

                    def steps(i, start, end):
                        for j in range(start, end):
                            at = unit_at(i, j + 2)
                            if at:
                                ii, u = at
                                b, qt = u // TB, u % TB
                                if qt == 0:
                                    wait(pe, qk_loaded[b], (ii + 1) * LOADS)
                                wait(pe, ttr_done, ii * NU + u - 1)
                                for c in range(2):
                                    mm = pe.matmul(psS[u % 2][:, c * CH:(c + 1) * CH], QA[b][:, qt * P:(qt + 1) * P],
                                                   KA[b][:, c * CH:(c + 1) * CH], start=True, stop=True)
                                mm.then_inc(s_done, 1)
                            at = unit_at(i, j)
                            if at and 0 <= j < NU:
                                ii, u = at
                                wait(pe, exp_done, ii * NU + u + 1)
                                for c in range(2):
                                    wait(pe, evac_done, (ii * NU + u) * 2 + c - 1)
                                    for t in range(4):
                                        mm = pe.transpose(psT[c][:, t, :], UU[u % 2][:, (4 * c + t) * P:(4 * c + t + 1) * P],
                                                          ident[:, :])
                                    mm.then_inc(t_done, 1)
                            q = j % GU
                            at = unit_at(i, j - 1 - q)
                            if group_end(at):
                                ii, u = at
                                b, g = u // TB, u // GU
                                if q == 0:
                                    wait(pe, evac_done, (ii * NU + u + 1) * 2)
                                    wait(pe, va_done, ii * B + b + 1)
                                    wait(pe, out_done, ii * NG + g - 1)
                                for kb in range(q * TB // GU, (q + 1) * TB // GU):
                                    mm = pe.matmul(psO[g % 2][0:DV + 1, :, :], VA[b][:, kb, :], PT[g % 2][:, kb, :, :],
                                                   start=kb == 0, stop=kb == TB - 1)
                                if q == GU - 1:
                                    mm.then_inc(pv_done, 1)
                            at = unit_at(i, j - 6)
                            if group_end(at):
                                ii, u = at
                                g = u // GU
                                wait(pe, os_done, ii * NG + g + 1)
                                for t in range(GU):
                                    mm = pe.transpose(psO[g % 2][:, t, 0:DV + 1], OS[g % 2][:, t, :],
                                                      ident[0:DV + 1, 0:DV + 1])
                                    if t == 0:
                                        mm.wait_op(s_done, 1, "sem-ge")
                                mm.then_inc(ot_done, 1)

                    passes(pe, steps)

                @blk.scalar
                def _(act):
                    act.wait_ge(ones_done, B)

                    def steps(i, start, end):
                        for j in range(start, end):
                            at = unit_at(i, j + 2)
                            if at:
                                ii, u = at
                                if u % TB == 0:
                                    b = u // TB
                                    wait(act, pv_done, (ii - 1) * NG + (b + 1) * (NG // B))
                                    act.copy(VA[b][:, :, 0:DV], V2[:, b * TB:(b + 1) * TB, bass.ds(ii * DV, DV)]
                                             ).then_inc(va_done, 1)
                                wait(act, s_done, ii * NU + u + 1)
                                wait(act, ttr_done, ii * NU + u - 1)
                                act.activation(RA[u % 2][:, :], psS[u % 2][:, :], ACT.Relu, scale=-0.8
                                               ).then_inc(relu_done, 1)
                            at = unit_at(i, j + 1)
                            if at and j >= -1:
                                ii, u = at
                                wait(act, ttr_done, ii * NU + u + 1)
                                act.activation(UU[u % 2][:, :], UU[u % 2][:, :], ACT.Exp, scale=-1.0,
                                               bias=nm[u % 2][:, 0:1]).then_inc(exp_done, 1)
                            at = unit_at(i, j - 5)
                            if group_end(at):
                                ii, u = at
                                g = u // GU
                                wait(act, pv_done, ii * NG + g + 1)
                                wait(act, ot_done, ii * NG + g - 1)
                                act.copy(OS[g % 2][:, :, :], psO[g % 2][0:DV + 1, :, :]).then_inc(os_done, 1)

                    passes(act, steps)

                @blk.vector
                def _(dve):
                    def steps(i, start, end):
                        for j in range(start, end):
                            at = unit_at(i, j + 1)
                            if at and j >= -1:
                                ii, u = at
                                wait(dve, relu_done, ii * NU + u + 1)
                                wait(dve, t_done, (ii * NU + u - 1) * 2)
                                wait(dve, exp_done, ii * NU + u - 1)
                                ins = dve.tensor_tensor_reduce(
                                    out=UU[u % 2][:, :], in0=psS[u % 2][:, :], in1=RA[u % 2][:, :], scale=-1.0,
                                    scalar=-NEG, op0=ALU.add, op1=ALU.min, accum_out=nm[u % 2][:, 0:1])
                                ins.wait_op(relu_done, 1, "sem-ge")
                                ins.then_inc(ttr_done, 1)
                            at = unit_at(i, j)
                            if at and 0 <= j < NU:
                                ii, u = at
                                g = u // GU
                                if u % GU == 0:
                                    wait(dve, pv_done, ii * NG + g - 1)
                                for c in range(2):
                                    wait(dve, t_done, (ii * NU + u) * 2 + c + 1)
                                    dve.tensor_copy(PT[g % 2][:, 4 * c:4 * c + 4, u % GU, :], psT[c][:, :, :]
                                                    ).then_inc(evac_done, 1)
                            at = unit_at(i, j - 6)
                            if group_end(at):
                                ii, u = at
                                g = u // GU
                                wait(dve, ot_done, ii * NG + g + 1)
                                dve.reciprocal(rl[g % 2][:, :], psO[g % 2][:, :, DV]).then_inc(rl_done, 1)
                                wait(dve, rl_done, ii * NG + g + 1)
                                dve.tensor_tensor(OB[:, g * GU:(g + 1) * GU, bass.ds(ii * DV, DV)],
                                                  psO[g % 2][:, :, 0:DV],
                                                  rl[g % 2][:, :].unsqueeze(2).broadcast_to([P, GU, DV]), ALU.mult
                                                  ).then_inc(out_done, 1)

                    passes(dve, steps)

            with ExitStack() as st:
                gam = tensor(st, "gam", [P, 1])
                s_g = sem(st, "s_g")
                s_s = sem(st, "s_s")
                blk = st.enter_context(nc.Block())

                @blk.sync
                def _(sp):
                    sp.dma_start(gam[:, :], gamma.rearrange("(a n) -> a n", a=1).broadcast_to([P, 1])).then_inc(s_g, 16)

                @blk.vector
                def _(dve):
                    dve.wait_ge(s_g, 16)
                    for c in range(4):
                        s = slice(4 * c, 4 * c + 4)
                        dve.scalar_tensor_tensor(out=A[:, s, :], in0=OB[:, s, :], scalar=gam[:, 0:1], in1=A[:, s, :],
                                                 op0=ALU.mult, op1=ALU.add).then_inc(s_s, 1)
                    for c in range(4):
                        s = slice(4 * c, 4 * c + 4)
                        dve.wait_ge(s_s, c + 1)
                        dve.tensor_tensor(X1[:, s, :], X[:, s, :], A[:, s, :], ALU.add)

        with ExitStack() as s3:
            WT = tensor(s3, "WT", [P, NT, E])
            Y = tensor(s3, "Y", [P, NT, D])
            WG = tensor(s3, "WG", [P, KD, E, M])
            WU = tensor(s3, "WU", [P, KD, E, M])
            WD = tensor(s3, "WD", [P, E, D])
            SG = tensor(s3, "SG", [P, KD, SM])
            SU = tensor(s3, "SU", [P, KD, SM])
            SD = tensor(s3, "SD", [P, SM // P, D])
            w_loaded = sem(s3, "w_loaded")
            N_W = 2 * KD + 4
            with ExitStack() as st:
                wt = tensor(st, "wt", [P, KD, E])
                wg = tensor(st, "wg", [G, E])
                cond_c = tensor(st, "cond_c", [G, B])
                cond_b = tensor(st, "cond_b", [G, B, P])
                lg = tensor(st, "lg", [P, B, E])
                L = tensor(st, "L", [P, NT, E])
                R1 = tensor(st, "R1", [P, NT])
                C1 = tensor(st, "C1", [P, NT, E, E])
                C2 = tensor(st, "C2", [P, NT, E, E])
                tri = tensor(st, "tri", [P, E, E])
                RK = tensor(st, "RK", [P, NT, E])
                s_w = sem(st, "s_w")
                s_tri = sem(st, "s_tri")
                s_tr = sem(st, "s_tr")
                s_ft = sem(st, "s_ft")
                s_cb = sem(st, "s_cb")
                s_l = sem(st, "s_l")
                s_dve = sem(st, "s_dve")
                s_mx = sem(st, "s_mx")
                s_ex = sem(st, "s_ex")
                psT = [psum(st, f"psT{i}", [P, CH]) for i in range(2)]
                psL = psum(st, "psL", [P, NT, E])
                psG = psum(st, "psG", [P, B, E])
                blk = st.enter_context(nc.Block())

                @blk.sync
                def _(sp):
                    sp.dma_start(wt[:, :, :], wtT.rearrange("(k p) n -> p k n", p=P)).then_inc(s_w, 16)
                    sp.dma_start(wg[:, :], wgT).then_inc(s_w, 16)
                    for b in range(B):
                        sp.dma_start(cond_c[:, b:b + 1], cond[b:b + 1, :].rearrange("a g -> g a")).then_inc(s_w, 16)
                    for k in range(KD):
                        sp.dma_start(WG[:, k], w_gate[:, k * P:(k + 1) * P, :].rearrange("e p m -> p e m")).then_inc(w_loaded, 16)
                        sp.dma_start(WU[:, k], w_up[:, k * P:(k + 1) * P, :].rearrange("e p m -> p e m")).then_inc(w_loaded, 16)
                    sp.dma_start(WD[:, :, :], w_down.rearrange("e p m -> p e m")).then_inc(w_loaded, 16)
                    for to, src in ((SG, sw_gate), (SU, sw_up), (SD, sw_down)):
                        sp.dma_start(to[:, :, :], src.rearrange("(k p) n -> p k n", p=P)).then_inc(w_loaded, 16)

                @blk.gpsimd
                def _(pool):
                    pool.memset(tri[:, :, :], 1.0).then_inc(s_tri, 1)
                    pool.wait_ge(s_tri, 1)
                    pool.affine_select(out=tri[:, :, :], in_=tri[:, :, :], compare_op=ALU.is_gt, fill=0.0, base=0,
                                       pattern=[[1, E], [-1, E]], channel_multiplier=0).then_inc(s_tri, 1)

                @blk.tensor
                def _(pe):
                    for c in range(NC_):
                        for k in range(KD):
                            n = c * KD + k
                            if n >= 2:
                                pe.wait_ge(s_ft, n - 1)
                            for t in range(4):
                                mm = pe.transpose(psT[n % 2][:, t * P:(t + 1) * P],
                                                  X1[:, 4 * c + t, k * P:(k + 1) * P], ident[:, :])
                            mm.then_inc(s_tr, 1)
                    pe.wait_ge(s_cb, B)
                    for b in range(B):
                        pe.matmul(psG[:, b, :], cond_b[:, b, :], wg[:, :], start=True, stop=True)
                    pe.wait_ge(s_ft, NC_ * KD)
                    for t in range(NT):
                        for k in range(KD):
                            mm = pe.matmul(psL[:, t, :], FT[:, k, t * P:(t + 1) * P], wt[:, k, :],
                                           start=k == 0, stop=k == KD - 1)
                    mm.then_inc(s_l, 1)

                @blk.scalar
                def _(act):
                    for c in range(NC_):
                        for k in range(KD):
                            n = c * KD + k
                            act.wait_ge(s_tr, n + 1)
                            act.copy(FT[:, k, c * CH:(c + 1) * CH], psT[n % 2][:, :]).then_inc(s_ft, 1)
                    act.wait_ge(s_mx, 1)
                    act.activation(L[:, :, :], L[:, :, :], ACT.Exp, scale=0.5).then_inc(s_ex, 1)

                @blk.vector
                def _(dve):
                    chain, after, count = own_results(dve, s_dve)
                    dve.wait_ge(s_w, 64)
                    for b in range(B):
                        dve.tensor_copy(cond_b[:, b, :], cond_c[:, b:b + 1].broadcast_to([G, P])).then_inc(s_cb, 1)
                    dve.wait_ge(s_l, 1)
                    chain(dve.tensor_copy(lg[:, :, :], psG[:, :, :]), True)
                    for b in range(B):
                        chain(dve.tensor_tensor(L[:, b * TB:(b + 1) * TB, :], psL[:, b * TB:(b + 1) * TB, :],
                                                lg[:, b:b + 1, :].broadcast_to([P, TB, E]), ALU.add))
                    after()
                    chain(dve.tensor_reduce(R1[:, :], L[:, :, :], AX_X, ALU.max), True)
                    dve.tensor_tensor(L[:, :, :], L[:, :, :], R1[:, :].unsqueeze(2).broadcast_to([P, NT, E]),
                                      ALU.subtract).then_inc(s_mx, 1)
                    dve.wait_ge(s_ex, 1)
                    chain(dve.tensor_reduce(R1[:, :], L[:, :, :], AX_X, ALU.add), True)
                    chain(dve.reciprocal(R1[:, :], R1[:, :]), True)
                    chain(dve.tensor_tensor(L[:, :, :], L[:, :, :], R1[:, :].unsqueeze(2).broadcast_to([P, NT, E]),
                                            ALU.mult), True)
                    mine = L[:, :, :].unsqueeze(3).broadcast_to([P, NT, E, E])
                    other = L[:, :, :].unsqueeze(2).broadcast_to([P, NT, E, E])
                    chain(dve.tensor_tensor(C1[:, :, :, :], other, mine, ALU.is_gt))
                    chain(dve.tensor_tensor(C2[:, :, :, :], other, mine, ALU.is_equal), True)
                    dve.wait_ge(s_tri, 2)
                    chain(dve.tensor_tensor(C2[:, :, :, :], C2[:, :, :, :],
                                            tri[:, :, :].unsqueeze(1).broadcast_to([P, NT, E, E]), ALU.mult), True)
                    chain(dve.tensor_tensor(C1[:, :, :, :], C1[:, :, :, :], C2[:, :, :, :], ALU.add), True)
                    chain(dve.tensor_reduce(RK[:, :, :], C1[:, :, :, :], AX_X, ALU.add), True)
                    chain(dve.scalar_tensor_tensor(out=L[:, :, :], in0=RK[:, :, :], scalar=2.0, in1=L[:, :, :],
                                                   op0=ALU.is_lt, op1=ALU.mult), True)
                    chain(dve.tensor_reduce(R1[:, :], L[:, :, :], AX_X, ALU.add), True)
                    chain(dve.tensor_scalar(R1[:, :], R1[:, :], 1e-20, None, ALU.add), True)
                    chain(dve.reciprocal(R1[:, :], R1[:, :]), True)
                    dve.tensor_tensor(WT[:, :, :], L[:, :, :], R1[:, :].unsqueeze(2).broadcast_to([P, NT, E]), ALU.mult)

            with ExitStack() as st:
                TT = CH // P
                JOBS = [("s", m) for m in range(SM // P)] + [("e", e) for e in range(E)]
                NJ = len(JOBS)
                NO = NJ - 1
                SA = [tensor(st, f"SA{i}", [P, CH]) for i in range(2)]
                LK = [tensor(st, f"LK{i}", [P, CH]) for i in range(2)]
                HH = [tensor(st, f"HH{i}", [P, CH]) for i in range(2)]
                psG = [psum(st, f"psG{i}", [P, CH]) for i in range(2)]
                psU = [psum(st, f"psU{i}", [P, CH]) for i in range(2)]
                psY = [psum(st, f"psY{i}", [P, TT, D]) for i in range(2)]
                gu_done = sem(st, "gu_done")
                sa_done = sem(st, "sa_done")
                lk_done = sem(st, "lk_done")
                hh_done = sem(st, "hh_done")
                down_done = sem(st, "down_done")
                y_done = sem(st, "y_done")
                y_init = sem(st, "y_init")
                blk = st.enter_context(nc.Block())

                def job_out(n):
                    o = max(n - 1, 0)
                    return o, n != 1, n != 0

                def chunks(eng, body):
                    body(0)
                    with eng.Fori(1, NC_) as i:
                        body(i)

                @blk.tensor
                def _(pe):
                    pe.wait_ge(w_loaded, 16 * N_W)

                    def body(i):
                        for n in range(NJ + 1):
                            if n < NJ:
                                kind, e = JOBS[n]
                                wait(pe, hh_done, i * NJ + n - 1)
                                for w, to in ((WG, psG), (WU, psU)):
                                    sw = SG if w is WG else SU
                                    for k in range(KD):
                                        wk = w[:, k, e, :] if kind == "e" else sw[:, k, e * P:(e + 1) * P]
                                        mm = pe.matmul(to[n % 2][:, :], wk, FT[:, k, bass.ds(i * CH, CH)],
                                                       start=k == 0, stop=k == KD - 1)
                                mm.then_inc(gu_done, 1)
                            if n >= 1:
                                kind, e = JOBS[n - 1]
                                o, first, last = job_out(n - 1)
                                wait(pe, hh_done, i * NJ + n)
                                if first:
                                    wait(pe, y_done, i * NO + o - 1)
                                for t in range(TT):
                                    mm = pe.matmul(psY[o % 2][:, t, :], HH[(n - 1) % 2][:, t * P:(t + 1) * P],
                                                   WD[:, e, :] if kind == "e" else SD[:, e, :],
                                                   start=first and t % 2 == 0, stop=last, skip_group_check=True)
                                mm.then_inc(down_done, 1)

                    chunks(pe, body)

                @blk.scalar
                def _(act):
                    def body(i):
                        for n in range(NJ):
                            wait(act, gu_done, i * NJ + n + 1)
                            wait(act, lk_done, i * NJ + n - 1)
                            act.activation(SA[n % 2][:, :], psG[n % 2][:, :], ACT.Copy, scale=0.01).then_inc(sa_done, 1)

                    chunks(act, body)

                @blk.vector
                def _(dve):
                    def body(i):
                        for n in range(NJ + 2):
                            if n < NJ:
                                wait(dve, sa_done, i * NJ + n + 1)
                                dve.tensor_tensor(LK[n % 2][:, :], psG[n % 2][:, :], SA[n % 2][:, :], ALU.max
                                                  ).then_inc(lk_done, 1)
                                wait(dve, lk_done, i * NJ + n + 1)
                                wait(dve, down_done, i * NJ + n - 1)
                                dve.tensor_tensor(HH[n % 2][:, :], psU[n % 2][:, :], LK[n % 2][:, :], ALU.mult
                                                  ).then_inc(hh_done, 1)
                            if n >= 2 and n - 1 >= 1:
                                m = n - 1
                                if m < NJ:
                                    kind, e = JOBS[m]
                                    wait(dve, down_done, i * NJ + m + 1)
                                    if m > 1:
                                        wait(dve, y_done, i * NO + m - 1)
                                    for t in range(TT):
                                        src = psY[(m - 1) % 2][:, t, :]
                                        dst = Y[:, bass.ds(i * TT + t, 1), :].rearrange("p a d -> p (a d)")
                                        if kind == "s":
                                            ins = dve.tensor_copy(dst, src)
                                        else:
                                            ins = dve.scalar_tensor_tensor(
                                                out=dst, in0=src,
                                                scalar=WT[:, bass.ds(i * TT + t, 1), e:e + 1].rearrange("p a d -> p (a d)"),
                                                in1=dst, op0=ALU.mult, op1=ALU.add)
                                    ins.then_inc(y_done, 1)

                    chunks(dve, body)

            with ExitStack() as st:
                wr_b = tensor(st, "wr_b", [P, D])
                WB = tensor(st, "WB", [P, KD, D])
                junk = tensor(st, "junk", [P, 4, N])
                SC = tensor(st, "SC", [P, NT])
                SW = tensor(st, "SW", [P, NT, P])
                SR = tensor(st, "SR", [P, B, N])
                low = tensor(st, "low", [P, P])
                cnt = tensor(st, "cnt", [P, NT, 3])
                sel = tensor(st, "sel", [P, NT])
                nsel = tensor(st, "nsel", [P, NT])
                GE = tensor(st, "GE", [P, NT, D])
                Z = tensor(st, "Z", [P, NT, D])
                s_w = sem(st, "s_w")
                s_low = sem(st, "s_low")
                s_tr = sem(st, "s_tr")
                s_ft = sem(st, "s_ft")
                s_sc = sem(st, "s_sc")
                s_sw = sem(st, "s_sw")
                s_st = sem(st, "s_st")
                s_sr = sem(st, "s_sr")
                s_cnt = sem(st, "s_cnt")
                s_dve = sem(st, "s_dve")
                s_h = sem(st, "s_h")
                s_ge = sem(st, "s_ge")
                s_z = sem(st, "s_z")
                s_out = sem(st, "s_out")
                psT = [psum(st, f"psT{i}", [P, CH]) for i in range(2)]
                psS = [psum(st, f"psS{i}", [P, CH]) for i in range(2)]
                psH = [psum(st, f"psH{i}", [P, CH]) for i in range(2)]
                blk = st.enter_context(nc.Block())

                @blk.sync
                def _(sp):
                    sp.dma_start(wr_b[:, :], w_router.rearrange("(a n) -> a n", a=1).broadcast_to([P, D])).then_inc(s_w, 16)
                    sp.dma_start(WB[:, :, :], w_block.rearrange("(k p) n -> p k n", p=P)).then_inc(s_w, 16)
                    ov = out.rearrange("b (t p) d -> p (b t) d", p=P)
                    for c in range(4):
                        sp.wait_ge(s_z, 4 * c + 4)
                        sp.dma_start(ov[:, 4 * c:4 * c + 4, :], Z[:, 4 * c:4 * c + 4, :]).then_inc(s_out, 16)
                    sp.wait_ge(s_out, 64)

                @blk.gpsimd
                def _(pool):
                    pool.memset(low[:, :], 1.0).then_inc(s_low, 1)
                    pool.wait_ge(s_low, 1)
                    pool.affine_select(out=low[:, :], in_=low[:, :], compare_op=ALU.is_gt, fill=0.0, base=0,
                                       pattern=[[-1, P]], channel_multiplier=1).then_inc(s_low, 1)

                @blk.tensor
                def _(pe):
                    for c in range(NC_):
                        for k in range(KD):
                            n = c * KD + k
                            if n >= 2:
                                pe.wait_ge(s_ft, n - 1)
                            for t in range(4):
                                mm = pe.transpose(psT[n % 2][:, t * P:(t + 1) * P],
                                                  Y[:, 4 * c + t, k * P:(k + 1) * P], ident[:, :])
                            mm.then_inc(s_tr, 1)
                    for c in range(NC_):
                        pe.wait_ge(s_sw, 4 * c + 4)
                        if c >= 2:
                            pe.wait_ge(s_sr, c - 1)
                        for t in range(4):
                            mm = pe.transpose(psS[c % 2][:, t * P:(t + 1) * P], SW[:, 4 * c + t, :], ident[:, :])
                        mm.then_inc(s_st, 1)
                    pe.wait_ge(s_ft, NC_ * KD)
                    pe.wait_ge(s_w, 32)
                    for t in range(NT):
                        if t >= 2:
                            pe.wait_ge(s_ge, t - 1)
                        for k in range(KD):
                            mm = pe.matmul(psH[t % 2][:, 0:D], FT[:, k, t * P:(t + 1) * P], WB[:, k, :],
                                           start=k == 0, stop=k == KD - 1)
                        mm.then_inc(s_h, 1)

                @blk.scalar
                def _(act):
                    for c in range(NC_):
                        for k in range(KD):
                            n = c * KD + k
                            act.wait_ge(s_tr, n + 1)
                            act.copy(FT[:, k, c * CH:(c + 1) * CH], psT[n % 2][:, :]).then_inc(s_ft, 1)
                    for c in range(NC_):
                        act.wait_ge(s_st, c + 1)
                        act.copy(SR[:, :, :].rearrange("p b n -> p (b n)")[:, c * CH:(c + 1) * CH], psS[c % 2][:, :]
                                 ).then_inc(s_sr, 1)
                    for t in range(NT):
                        act.wait_ge(s_h, t + 1)
                        act.activation(GE[:, t, :], psH[t % 2][:, 0:D], ACT.Gelu_apprx_tanh).then_inc(s_ge, 1)

                @blk.vector
                def _(dve):
                    chain, after, count = own_results(dve, s_dve)
                    dve.wait_ge(s_w, 32)
                    for t in range(NT):
                        dve.tensor_tensor_reduce(out=Z[:, t, :], in0=Y[:, t, :], in1=wr_b[:, :], scale=1.0, scalar=0.0,
                                                 op0=ALU.mult, op1=ALU.add, accum_out=SC[:, t:t + 1]).then_inc(s_sc, 1)
                    for t in range(NT):
                        dve.wait_ge(s_sc, t + 1)
                        dve.tensor_copy(SW[:, t, :], SC[:, t:t + 1].broadcast_to([P, P])).then_inc(s_sw, 1)
                    chain(dve.memset(cnt[:, :, :], 0.0), True)
                    dve.wait_ge(s_low, 2)
                    for t in range(NT):
                        b, q = t // TB, t % TB
                        mine = SC[:, t:t + 1]
                        dve.wait_ge(s_sr, (b + 1) * (N // CH))
                        if q > 0:
                            after(3)
                            chain(dve.tensor_scalar(junk[:, count[0] % 4, 0:q * P], SR[:, b, 0:q * P], mine, 0.0,
                                                    ALU.is_ge, ALU.add, accum_out=cnt[:, t, 0:1]))
                        after(3)
                        chain(dve.tensor_scalar(junk[:, count[0] % 4, 0:N - q * P], SR[:, b, q * P:N], mine, 0.0,
                                                ALU.is_gt, ALU.add, accum_out=cnt[:, t, 1:2]))
                        after(3)
                        chain(dve.scalar_tensor_tensor(out=junk[:, count[0] % 4, 0:P], in0=SR[:, b, q * P:(q + 1) * P],
                                                       scalar=mine, in1=low[:, :], op0=ALU.is_equal, op1=ALU.mult,
                                                       accum_out=cnt[:, t, 2:3]))
                    after()
                    chain(dve.tensor_reduce(sel[:, :], cnt[:, :, :], AX_X, ALU.add), True)
                    chain(dve.tensor_scalar(nsel[:, :], sel[:, :], float(TOPK), None, ALU.is_ge), True)
                    chain(dve.tensor_scalar(sel[:, :], sel[:, :], float(TOPK), None, ALU.is_lt), True)
                    for t in range(NT):
                        dve.wait_ge(s_ge, t + 1)
                        chain(dve.scalar_tensor_tensor(out=Z[:, t, :], in0=GE[:, t, :], scalar=sel[:, t:t + 1],
                                                       in1=X1[:, t, :], op0=ALU.mult, op1=ALU.add))
                    after()
                    for t in range(NT):
                        dve.scalar_tensor_tensor(out=Z[:, t, :], in0=Y[:, t, :], scalar=nsel[:, t:t + 1],
                                                 in1=Z[:, t, :], op0=ALU.mult, op1=ALU.add).then_inc(s_z, 1)


_NAMES = {"x": "x", "fside_16xSxS_0": "bias1", "cond_64": "cond", "mask_BxS_bk0": "mask", "L0_cond_g_in": "g_in",
          "L0_cond_null_attn_bias": "null_bias", "L0_cond_Wq": "wq1", "L0_cond_Wkv": "wkv1", "L0_cond_Wo": "wo1",
          "L0_cond_g_out": "g_out", "L0_attn_Wq": "wq2T", "L0_attn_bq": "bq2", "L0_attn_Wk": "wk2T",
          "L0_attn_bk": "bk2", "L0_attn_Wv": "wv2T", "L0_attn_bv": "bv2", "L0_attn_gamma": "gamma",
          "L0_cond2_wt": "wtT", "L0_cond2_wg": "wgT", "L0_cond2_w_gate": "w_gate", "L0_cond2_w_up": "w_up",
          "L0_cond2_w_down": "w_down", "L0_cond2_sw_gate": "sw_gate", "L0_cond2_sw_up": "sw_up",
          "L0_cond2_sw_down": "sw_down", "L0_ffn_w_router": "w_router", "L0_ffn_w_block": "w_block"}


def kernel(**inputs):
    import numpy as np
    import concourse.bacc as bacc
    from concourse.bass_utils import run_bass_kernel_spmd

    nc = bacc.Bacc("TRN2", target_bir_lowering=False, num_devices=1)
    arrays, args = {}, {}
    for name, short in _NAMES.items():
        a = np.asarray(inputs[name])
        if short.endswith("T"):
            a = a.T
        a = np.ascontiguousarray(a)
        if a.dtype == np.bool_:
            a = a.view(np.int32)
        arrays["in_" + short] = a
        args[short] = nc.dram_tensor("in_" + short, a.shape, mybir.dt.from_np(a.dtype), kind="ExternalInput").ap()
    out = nc.dram_tensor("out_dram", (B, N, D), F32, kind="ExternalOutput").ap()
    program(nc, out=out, **args)
    r = run_bass_kernel_spmd(nc, [arrays], core_ids=[0])
    return r.results[0]["out_dram"]
```
